# Optimizing a Trainium2 kernel written in Bass

```python
import numpy as np
import jax
import jax.numpy as jnp

def _softmax(x, axis=-1):
    return jax.nn.softmax(x, axis=axis)

def _gelu(x):
    return jax.nn.gelu(x, approximate=True)

def _silu(x):
    return jax.nn.silu(x)

def _sigmoid(x):
    return jax.nn.sigmoid(x)

def _layernorm(x, axis=-1, eps=1e-05):
    m = jnp.mean(x, axis=axis, keepdims=True)
    v = jnp.var(x, axis=axis, keepdims=True)
    return (x - m) / jnp.sqrt(v + eps)

def _scatter_add(tgt, idx, src, axis=0):
    return tgt.at[idx].add(src)

def _segment_sum(src, seg, n):
    return jax.ops.segment_sum(src, seg, n)
kernel_name = 'mk_sandwich_d1_jaxref_r8_822679'

def setup_inputs(seed: int=0):
    np.random.seed(seed)
    _w = jnp.asarray

    def _L0_attn_setup():
        import jax, jax.numpy as jnp
        import numpy as np
        B, SEQ, DIM = (2, 256, 512)
        N_HEADS, N_KV_HEADS, HEAD_DIM = (32, 8, 128)
        N_REP = N_HEADS // N_KV_HEADS
        ROPE_THETA = 10000.0

        def _rope_cos_sin(seq_len, head_dim, theta):
            inv_freq = 1.0 / theta ** (jnp.arange(0, head_dim, 2, dtype=jnp.float32) / head_dim)
            ang = jnp.arange(seq_len, dtype=jnp.float32)[:, None] * inv_freq[None, :]
            return (jnp.cos(ang), jnp.sin(ang))

        def _apply_rope(x, cos, sin):
            xr = x[..., 0::2]
            xi = x[..., 1::2]
            c = cos[None, :, None, :]
            s = sin[None, :, None, :]
            out_r = xr * c - xi * s
            out_i = xr * s + xi * c
            return jnp.stack([out_r, out_i], axis=-1).reshape(x.shape)
        key = jax.random.key(seed)
        k0, k1, k2, k3, k4 = jax.random.split(key, 5)
        return {'x': jax.random.normal(k0, (B, SEQ, DIM), jnp.float32), 'wq': jax.random.normal(k1, (DIM, N_HEADS * HEAD_DIM), jnp.float32) * 0.02, 'wk': jax.random.normal(k2, (DIM, N_KV_HEADS * HEAD_DIM), jnp.float32) * 0.02, 'wv': jax.random.normal(k3, (DIM, N_KV_HEADS * HEAD_DIM), jnp.float32) * 0.02, 'wo': jax.random.normal(k4, (N_HEADS * HEAD_DIM, DIM), jnp.float32) * 0.02}
    _L0_attn_in = _L0_attn_setup()

    def _L0_ffn_setup():
        import jax, jax.numpy as jnp
        import numpy as np
        FP4_E2_GRID = jnp.array([-6.0, -4.0, -3.0, -2.0, -1.5, -1.0, -0.5, 0.0, 0.5, 1.0, 1.5, 2.0, 3.0, 4.0, 6.0], dtype=jnp.float32)
        GRID_ABS_MAX = 6.0
        GROUP_SIZE = 128

        def _nearest_grid(xs):
            idx = jnp.argmin(jnp.abs(xs[..., None] - FP4_E2_GRID), axis=-1)
            return FP4_E2_GRID[idx]

        def fp4_e2_quant_per_token(x):
            x = jnp.clip(x, -3.0, 3.0)
            scale = jnp.max(jnp.abs(x), axis=-1, keepdims=True) / GRID_ABS_MAX
            return _nearest_grid(x / scale) * scale

        def fp4_e2_quant_per_group(w, group_size=GROUP_SIZE):
            w_shape = w.shape
            wg = w.reshape(-1, group_size)
            scale = jnp.max(jnp.abs(wg), axis=-1, keepdims=True) / GRID_ABS_MAX
            return (_nearest_grid(wg / scale) * scale).reshape(w_shape)
        key = jax.random.key(seed)
        k1, k2, k3 = jax.random.split(key, 3)
        x = jax.random.normal(k1, (2, 128, 512), dtype=jnp.float32)
        weight = jax.random.normal(k2, (512, 512), dtype=jnp.float32) * 0.02
        bias = jax.random.normal(k3, (512,), dtype=jnp.float32) * 0.02
        return {'x': x, 'weight': weight, 'bias': bias}
    _L0_ffn_in = _L0_ffn_setup()
    _d = {'L0_attn_x': _L0_attn_in['x'], 'L0_attn_wq': _L0_attn_in['wq'], 'L0_attn_wk': _L0_attn_in['wk'], 'L0_attn_wv': _L0_attn_in['wv'], 'L0_attn_wo': _L0_attn_in['wo'], 'L0_ffn_weight': _L0_ffn_in['weight'], 'L0_ffn_bias': _L0_ffn_in['bias']}
    _x0 = _d['L0_attn_x']
    _d['L0_attn_x'] = jax.random.normal(jax.random.fold_in(jax.random.key(seed), 1), (1, 1024, 512), dtype=_x0.dtype)
    del _x0
    return _d

def reference(L0_attn_x, L0_attn_wq, L0_attn_wk, L0_attn_wv, L0_attn_wo, L0_ffn_weight, L0_ffn_bias):

    def _L0_attn_ref(x, wq, wk, wv, wo):
        import jax, jax.numpy as jnp
        import numpy as np
        B, SEQ, DIM = (2, 256, 512)
        N_HEADS, N_KV_HEADS, HEAD_DIM = (32, 8, 128)
        N_REP = N_HEADS // N_KV_HEADS
        ROPE_THETA = 10000.0

        def _rope_cos_sin(seq_len, head_dim, theta):
            inv_freq = 1.0 / theta ** (jnp.arange(0, head_dim, 2, dtype=jnp.float32) / head_dim)
            ang = jnp.arange(seq_len, dtype=jnp.float32)[:, None] * inv_freq[None, :]
            return (jnp.cos(ang), jnp.sin(ang))

        def _apply_rope(x, cos, sin):
            xr = x[..., 0::2]
            xi = x[..., 1::2]
            c = cos[None, :, None, :]
            s = sin[None, :, None, :]
            out_r = xr * c - xi * s
            out_i = xr * s + xi * c
            return jnp.stack([out_r, out_i], axis=-1).reshape(x.shape)
        bsz, seq_len, _ = x.shape
        xq = (x @ wq).reshape(bsz, seq_len, N_HEADS, HEAD_DIM)
        xk = (x @ wk).reshape(bsz, seq_len, N_KV_HEADS, HEAD_DIM)
        xv = (x @ wv).reshape(bsz, seq_len, N_KV_HEADS, HEAD_DIM)
        cos, sin = _rope_cos_sin(seq_len, HEAD_DIM, ROPE_THETA)
        xq = _apply_rope(xq, cos, sin)
        xk = _apply_rope(xk, cos, sin)
        keys = jnp.repeat(xk, N_REP, axis=2)
        values = jnp.repeat(xv, N_REP, axis=2)
        xq_t = xq.transpose(0, 2, 1, 3)
        k_t = keys.transpose(0, 2, 1, 3)
        v_t = values.transpose(0, 2, 1, 3)
        scores = jnp.einsum('bhqd,bhkd->bhqk', xq_t, k_t) / jnp.sqrt(jnp.float32(HEAD_DIM))
        q_idx = jnp.arange(seq_len)
        mask = jnp.where(q_idx[None, :] > q_idx[:, None], -jnp.inf, 0.0).astype(scores.dtype)
        scores = scores + mask[None, None, :, :]
        attn = jax.nn.softmax(scores.astype(jnp.float32), axis=-1).astype(xq_t.dtype)
        out = jnp.einsum('bhqk,bhkd->bhqd', attn, v_t)
        out = out.transpose(0, 2, 1, 3).reshape(bsz, seq_len, N_HEADS * HEAD_DIM)
        return out @ wo

    def _L0_ffn_ref(x, weight, bias):
        import jax, jax.numpy as jnp
        import numpy as np
        FP4_E2_GRID = jnp.array([-6.0, -4.0, -3.0, -2.0, -1.5, -1.0, -0.5, 0.0, 0.5, 1.0, 1.5, 2.0, 3.0, 4.0, 6.0], dtype=jnp.float32)
        GRID_ABS_MAX = 6.0
        GROUP_SIZE = 128

        def _nearest_grid(xs):
            idx = jnp.argmin(jnp.abs(xs[..., None] - FP4_E2_GRID), axis=-1)
            return FP4_E2_GRID[idx]

        def fp4_e2_quant_per_token(x):
            x = jnp.clip(x, -3.0, 3.0)
            scale = jnp.max(jnp.abs(x), axis=-1, keepdims=True) / GRID_ABS_MAX
            return _nearest_grid(x / scale) * scale

        def fp4_e2_quant_per_group(w, group_size=GROUP_SIZE):
            w_shape = w.shape
            wg = w.reshape(-1, group_size)
            scale = jnp.max(jnp.abs(wg), axis=-1, keepdims=True) / GRID_ABS_MAX
            return (_nearest_grid(wg / scale) * scale).reshape(w_shape)
        w_q = fp4_e2_quant_per_group(weight)
        x_q = fp4_e2_quant_per_token(x)
        return jnp.einsum('bsi,oi->bso', x_q, w_q) + bias
    x = L0_attn_x
    x = x + _layernorm(_L0_attn_ref(_layernorm(x, axis=-1), L0_attn_wq, L0_attn_wk, L0_attn_wv, L0_attn_wo), axis=-1)
    x = x + _layernorm(_L0_ffn_ref(_layernorm(x, axis=-1), L0_ffn_weight, L0_ffn_bias), axis=-1)
    return x

_drawn_inputs = setup_inputs


def setup_inputs(seed=0):
    import zlib

    import numpy as np

    out = dict(_drawn_inputs(seed))
    spreads = {}
    factors = {}
    for name, (base, spread) in spreads.items():
        noise = np.random.default_rng([zlib.crc32(name.encode()), seed]).standard_normal(out[name].shape)
        drawn = base * np.exp(spread * noise) if base else spread * noise
        out[name] = jnp.asarray(drawn.astype(out[name].dtype))
    for name, factor in factors.items():
        out[name] = (out[name] * factor).astype(out[name].dtype)
    return out
```

```python
from contextlib import ExitStack

import numpy as np

import concourse.bass as bass
from concourse import mybir


P = 128
SEQ, DIM = 1024, 512
HEADS, KV_HEADS = 32, 8
REP = HEADS // KV_HEADS
TILES = SEQ // P
KT = DIM // P
QW = REP * P
QKW = QW + P
QKVW = QKW + P
BANK = 512
LN_EPS = 1e-5
MASKED = -3.0e38

GRID = [-6.0, -4.0, -3.0, -2.0, -1.5, -1.0, -0.5, 0.0, 0.5, 1.0, 1.5, 2.0, 3.0, 4.0, 6.0]
THRESHOLD = [(a + b) / 2 for a, b in zip(GRID, GRID[1:])]
STEP = [b - a for a, b in zip(GRID, GRID[1:])]
NT = len(STEP)
GRID_MAX = 6.0
CLIP = 3.0
STEPS = [0.5, 1.0, 2.0]

F32 = mybir.dt.float32
F32R = mybir.dt.float32r
BF16 = mybir.dt.bfloat16
ALU = mybir.AluOpType
ACT = mybir.ActivationFunctionType
AX = mybir.AxisListType

BLOCKS = [(t, j) for t in range(TILES) for j in range(t + 1)]
NB = len(BLOCKS)
FIRST_BLOCK = [BLOCKS.index((t, 0)) for t in range(TILES)] + [NB]
UNITS = TILES * REP
E_USES = 2 * TILES + NB
CHUNKS = KT + REP
STAGED = 2 * (3 * 16) + 2 * 16


def attention_order():
    order = [("S", 0, h) for h in range(REP)]
    for t in range(TILES):
        if t + 1 < TILES:
            fill = [("S", t + 1, h) for h in range(REP)]
        else:
            fill = [("P", 0), ("P", 1)]
        order.append(fill.pop(0))
        if t == 0:
            order.append(("C", TILES - 1, "own"))
        else:
            order.append(("W", t - 1))
        order.append(fill.pop(0))
        n = t + 1
        for j in range(n):
            order.append(("E", FIRST_BLOCK[t] + j))
            while fill and len(fill) * n >= 2 * (n - j):
                order.append(fill.pop(0))
            if j:
                order.append(("PV", FIRST_BLOCK[t] + j - 1))
        order += fill
        order.append(("PV", FIRST_BLOCK[t] + n - 1))
    return order


def projection_order(after_attention):
    order = [("V", 0), ("V", 1), ("W", TILES - 1)] if after_attention else [("P", 0), ("V", 0), ("P", 1), ("V", 1)]
    for t in range(2, TILES):
        order += [("C", t - 2), ("P", t), ("V", t)]
    return order + [("C", TILES - 2)]


def rope_tables():
    half = np.arange(0, P, 2, dtype=np.float32) / np.float32(P)
    inv_freq = np.float32(1.0) / np.power(np.float32(10000.0), half)
    angle = np.arange(SEQ, dtype=np.float32)[:, None] * inv_freq[None, :]
    root = float(P) ** -0.25
    cos = np.cos(angle.astype(np.float64)) * root
    sin = np.sin(angle.astype(np.float64)) * root
    signed = np.stack([-sin, sin], axis=-1).reshape(SEQ, P)
    return cos.astype(np.float32), signed.astype(np.float32)


def shape_constants():
    causal = np.where(np.arange(P)[None, :] > np.arange(P)[:, None], MASKED, 0.0).astype(np.float32)
    cos, sin = rope_tables()
    thresholds = np.broadcast_to(np.array(THRESHOLD, np.float32), (P, NT)).copy()
    return {"cos": cos, "sin": sin, "causal": causal, "eye": np.eye(P, dtype=np.float32),
            "thresholds": thresholds}


def sandwich_kernel(nc, x, wq, wk, wv, wo, ffn_w, ffn_b, cos, sin, causal, eye, thresholds, out):
    ctx = ExitStack()
    with ctx:
        def sb(name, shape, dt=F32):
            return ctx.enter_context(nc.sbuf_tensor(name, shape, dt))

        def pb(name, shape):
            return ctx.enter_context(nc.psum_tensor(name, shape, F32))

        def sem(name):
            return ctx.enter_context(nc.semaphore(name))

        cos_t = sb("cos_t", [P, TILES, P // 2])
        sin_t = sb("sin_t", [P, TILES, P])
        stage = sb("stage", [P, 2, QKVW])
        wqkv_hi = sb("wqkv_hi", [P, KT, QKVW], F32R)
        wqkv_lo = sb("wqkv_lo", [P, KT, QKVW], F32R)
        wo_hi = sb("wo_hi", [P, REP, DIM], F32R)
        wo_lo = sb("wo_lo", [P, REP, DIM], F32R)
        rope_a = sb("rope_a", [P, 2, QKW])
        rope_b = sb("rope_b", [P, 2, QKW])
        qT_hi = sb("qT_hi", [P, REP, SEQ], F32R)
        qT_lo = sb("qT_lo", [P, REP, SEQ], F32R)
        kT_hi = sb("kT_hi", [P, SEQ], F32R)
        kT_lo = sb("kT_lo", [P, SEQ], F32R)
        v_hi = sb("v_hi", [P, TILES, P], F32R)
        v_lo = sb("v_lo", [P, TILES, P], F32R)
        probs_mem = sb("probs_mem", [P, REP * (2 * TILES - 1) * P])
        probs = [probs_mem[:, 0:REP * (TILES - 1) * P].rearrange("p (h k) -> p h k", h=REP),
                 probs_mem[:, REP * (TILES - 1) * P:].rearrange("p (h k) -> p h k", h=REP)]
        pT_hi = sb("pT_hi", [P, 2, QW], F32R)
        pT_lo = sb("pT_lo", [P, 2, QW], F32R)
        oT_hi = sb("oT_hi", [P, 2, QW], F32R)
        oT_lo = sb("oT_lo", [P, 2, QW], F32R)
        y_acc = sb("y_acc", [P, TILES, DIM])
        eye_f = sb("eye_f", [P, P])
        eye_b = sb("eye_b", [P, len(STEPS), P], BF16)
        causal_b = sb("causal_b", [P, P], BF16)
        thr = sb("thr", [P, NT])
        neg_max = sb("neg_max", [P, 8])
        row_sum = sb("row_sum", [P, 8])
        row_inv = sb("row_inv", [P, 8])
        stats = sb("stats", [P, 6])
        mean_var = sb("mean_var", [P, 2])
        var_eps = sb("var_eps", [P, 1])
        rstd = sb("rstd", [P, 1])
        minus_half = sb("minus_half", [P, 1])
        s_max = sb("s_max", [P, 16])
        s_q = sb("s_q", [P, 16])
        s_e = sb("s_e", [P, 16])
        scale = sb("scale", [P, 16])
        thr_s = sb("thr_s", [P, NT])

        x_sb = probs_mem[:, 0:TILES * DIM].rearrange("p (t d) -> p t d", t=TILES)
        causal_f = rope_b[:, 0, 0:P]
        wT_hi = wqkv_hi[:, :, 0:DIM]
        wT_lo = wqkv_lo[:, :, 0:DIM]
        xn2 = rope_a[:, 0, 0:DIM]
        bias_b = rope_a[:, 1, 0:DIM]
        xg_T = pT_hi[:, 0, :]
        z_sb = rope_b[:, 0, 0:DIM]
        res = stage[:, :, 0:DIM]

        with nc.sbuf_tensor("xT_hi", [P, KT, SEQ], F32R) as xT_hi, nc.sbuf_tensor("xT_lo", [P, KT, SEQ], F32R) as xT_lo:
            pass
        w_raw = sb("w_raw", [P, 4, DIM])
        w_quant = sb("w_quant", [P, 4, DIM])
        above = sb("above", [P, NT, DIM], BF16)
        w_above = above[:, 0:8, :].rearrange("p (n m) d -> p n (m d)", n=2)

        ps_s = pb("ps_s", [P, 2, 2 * BANK])
        ps_e = pb("ps_e", [P, 2, BANK])
        ps_o = pb("ps_o", [P, BANK])
        ps_y = pb("ps_y", [P, BANK])

        const_loaded = sem("const_loaded")
        x_loaded = [sem("x_first_loaded"), sem("x_rest_loaded")]
        const_made = sem("const_made")
        ln_step = sem("ln_step")
        ln_rstd = sem("ln_rstd")
        ln_var = sem("ln_var")
        xn_ready = sem("xn_ready")
        xT_done = sem("xT_done")
        xT_hi_done = sem("xT_hi_done")
        xT_lo_done = sem("xT_lo_done")
        staged = [sem("staged0"), sem("staged1")]
        stage_free = sem("stage_free")
        split_hi = sem("split_hi")
        pool_turns = sem("pool_turns")
        wqkv_ready = sem("wqkv_ready")
        wo_ready = sem("wo_ready")
        proj_done = sem("proj_done")
        rope_mul = sem("rope_mul")
        rope_sum = sem("rope_sum")
        v_hi_done = sem("v_hi_done")
        qkv_free = sem("qkv_free")
        qkT_done = sem("qkT_done")
        qkT_hi_done = sem("qkT_hi_done")
        e_free = sem("e_free")
        scores_done = sem("scores_done")
        max_done = sem("max_done")
        exp_done = sem("exp_done")
        inv_done = sem("inv_done")
        probs_ready = sem("probs_ready")
        pT_done = sem("pT_done")
        pT_hi_done = sem("pT_hi_done")
        pv_done = sem("pv_done")
        oT_hi_done = sem("oT_hi_done")
        oT_lo_done = sem("oT_lo_done")
        y_done = sem("y_done")
        y_added = sem("y_added")
        ffn_loaded = sem("ffn_loaded")
        f_chain = sem("f_chain")
        w_above_done = sem("w_above_done")
        w_sum_done = sem("w_sum_done")
        w_quant_done = sem("w_quant_done")
        wT_done = sem("wT_done")
        wT_hi_done = sem("wT_hi_done")
        wT_lo_done = sem("wT_lo_done")
        above_done = sem("above_done")
        xgT_done = sem("xgT_done")
        xgT_copied = sem("xgT_copied")
        z_done = sem("z_done")
        z_read = sem("z_read")
        res_ready = sem("res_ready")
        stored = [sem("stored_even"), sem("stored_odd")]

        block = ctx.enter_context(nc.Block())
        x_v = x[0].rearrange("(t p) d -> p t d", p=P)
        out_v = out[0].rearrange("(t p) d -> p t d", p=P)

        @block.sync
        def _(sp):
            def load_qkv(G, kt):
                n = CHUNKS * G + kt
                if not (isinstance(G, int) and n < 2):
                    sp.wait_ge(stage_free, n - 1)
                rows = slice(kt * P, (kt + 1) * P)
                b = kt % 2
                sp.dma_start(stage[:, b, 0:QW], wq[rows, bass.ds(G * QW, QW)]).then_inc(staged[b], 16)
                sp.dma_start(stage[:, b, QW:QKW], wk[rows, bass.ds(G * P, P)]).then_inc(staged[b], 16)
                sp.dma_start(stage[:, b, QKW:QKVW], wv[rows, bass.ds(G * P, P)]).then_inc(staged[b], 16)

            def load_wo(G, h):
                sp.wait_ge(stage_free, CHUNKS * G + KT + h - 1)
                sp.dma_start(stage[:, h % 2, 0:DIM], wo[bass.ds(G * QW + h * P, P), :]).then_inc(staged[h % 2], 16)

            sp.dma_start(x_sb[:, 0, :], x_v[:, 0, :]).then_inc(x_loaded[0], 16)
            sp.dma_start(x_sb[:, 1:, :], x_v[:, 1:, :]).then_inc(x_loaded[1], 16)
            sp.dma_start(eye_f[:, :], eye).then_inc(const_loaded, 16)
            sp.dma_start(causal_f, causal).then_inc(const_loaded, 16)
            sp.dma_start(thr[:, :], thresholds).then_inc(const_loaded, 16)
            for kt in range(2):
                load_qkv(0, kt)
            sp.dma_start(cos_t[:, :, :], cos.rearrange("(t p) d -> p t d", p=P)).then_inc(const_loaded, 16)
            sp.dma_start(sin_t[:, :, :], sin.rearrange("(t p) d -> p t d", p=P)).then_inc(const_loaded, 16)
            for kt in range(2, KT):
                load_qkv(0, kt)
            for h in range(REP):
                load_wo(0, h)
            with sp.Fori(0, KV_HEADS - 1) as g:
                for kt in range(KT):
                    load_qkv(g + 1, kt)
                for h in range(REP):
                    load_wo(g + 1, h)
            sp.wait_ge(y_done, TILES * KV_HEADS)
            sp.dma_start(w_raw[:, :, :], ffn_w.rearrange("(r p) i -> p r i", p=P)).then_inc(ffn_loaded, 16)
            sp.dma_start(x_sb, x_v).then_inc(ffn_loaded, 16)
            sp.dma_start(bias_b, ffn_b.rearrange("(a d) -> a d", a=1).to_broadcast([P, DIM])).then_inc(ffn_loaded, 16)
            for t in range(TILES):
                sp.wait_ge(res_ready, t + 1)
                sp.dma_start(out_v[:, t, :], res[:, t % 2, :]).then_inc(stored[t % 2], 16)
            for done in stored:
                sp.wait_ge(done, 16 * TILES // 2)

        @block.tensor
        def _(pe):
            def transpose_x(t):
                pe.wait_ge(xn_ready, t + 1)
                if t >= 2:
                    pe.wait_ge(xT_lo_done, t - 1)
                bank = ps_o if t % 2 == 0 else ps_y
                for kt in range(KT):
                    last = nc.tensor.transpose(bank[:, kt * P:(kt + 1) * P], x_sb[:, t, kt * P:(kt + 1) * P], eye_f[:, :])
                last.then_inc(xT_done, 1)

            def project(G, t):
                first = isinstance(G, int) and G == 0
                if first:
                    pe.wait_ge(xT_lo_done, t + 1)
                if t == 0 and not first:
                    pe.wait_ge(wqkv_ready, KT * G + KT)
                if t >= 2:
                    pe.wait_ge(qkv_free, TILES * G + t - 1)
                elif not first:
                    pe.wait_ge(exp_done, UNITS * G - 1 + t)
                s = t % 2
                rows = slice(t * P, (t + 1) * P)
                n = 0
                for kt in range(KT):
                    if t == 0 and first:
                        pe.wait_ge(wqkv_ready, kt + 1)
                    for a, b in ((xT_hi, wqkv_hi), (xT_hi, wqkv_lo), (xT_lo, wqkv_hi)):
                        n += 1
                        nc.tensor.matmul(ps_s[:, s, 0:QW], a[:, kt, rows], b[:, kt, 0:QW],
                                         start=n == 1, stop=n == 3 * KT)
                        last = nc.tensor.matmul(ps_s[:, s, QW:QKVW], a[:, kt, rows], b[:, kt, QW:QKVW],
                                                start=n == 1, stop=n == 3 * KT)
                last.then_inc(proj_done, 1)

            def transpose_qk(G, t):
                pe.wait_ge(rope_sum, TILES * G + t + 1)
                n = E_USES * G + 2 * t
                if not (isinstance(G, int) and n == 0):
                    pe.wait_ge(e_free, n)
                for h in range(REP):
                    nc.tensor.transpose(ps_e[:, 0, h * P:(h + 1) * P], rope_a[:, t % 2, h * P:(h + 1) * P], eye_f[:, :])
                nc.tensor.transpose(ps_e[:, 1, 0:P], rope_a[:, t % 2, QW:QKW], eye_f[:, :]).then_inc(qkT_done, 1)

            def score(G, t, h):
                u = REP * t + h
                s = u % 2
                if h == 0:
                    pe.wait_ge(e_free, E_USES * G + 2 * t + 2)
                if u >= 2:
                    pe.wait_ge(exp_done, UNITS * G + u - 1)
                else:
                    pe.wait_ge(qkv_free, TILES * G + TILES - 1 + u)
                q_rows = slice(t * P, (t + 1) * P)
                width = (t + 1) * P
                for c0 in range(0, width, BANK):
                    c1 = min(c0 + BANK, width)
                    nc.tensor.matmul(ps_s[:, s, c0:c1], qT_hi[:, h, q_rows], kT_hi[:, c0:c1], start=True, stop=False)
                    nc.tensor.matmul(ps_s[:, s, c0:c1], qT_hi[:, h, q_rows], kT_lo[:, c0:c1], start=False, stop=False)
                    nc.tensor.matmul(ps_s[:, s, c0:c1], qT_lo[:, h, q_rows], kT_hi[:, c0:c1], start=False,
                                     stop=c1 < width)
                nc.tensor.matmul(ps_s[:, s, t * P:width], eye_b[:, 1, :], causal_b[:, :], start=False,
                                 stop=True).then_inc(scores_done, 1)

            def transpose_probs(G, b):
                t, j = BLOCKS[b]
                if j == 0:
                    pe.wait_ge(probs_ready, UNITS * G + REP * (t + 1))
                pe.wait_ge(e_free, E_USES * G + 2 * TILES + b - 1)
                for h in range(REP):
                    last = nc.tensor.transpose(ps_e[:, b % 2, h * P:(h + 1) * P], probs[t % 2][:, h, j * P:(j + 1) * P],
                                               eye_f[:, :])
                last.then_inc(pT_done, 1)

            def values(G, b):
                t, j = BLOCKS[b]
                if j == 0:
                    pe.wait_ge(oT_lo_done, TILES * G + t + 1)
                pe.wait_ge(e_free, E_USES * G + 2 * TILES + b + 1)
                nc.tensor.matmul(ps_o[:, :], v_hi[:, j, :], pT_hi[:, b % 2, :], start=j == 0, stop=False)
                nc.tensor.matmul(ps_o[:, :], v_lo[:, j, :], pT_hi[:, b % 2, :], start=False, stop=False)
                nc.tensor.matmul(ps_o[:, :], v_hi[:, j, :], pT_lo[:, b % 2, :], start=False,
                                 stop=j == t).then_inc(pv_done, 1)

            def project_out(G, t):
                if t == 0:
                    pe.wait_ge(wo_ready, REP * G + REP)
                pe.wait_ge(y_added, TILES * G + t + 1)
                pe.wait_ge(oT_lo_done, TILES * G + t + 2)
                n = 0
                for h in range(REP):
                    head = slice(h * P, (h + 1) * P)
                    for a, b in ((oT_hi, wo_hi), (oT_hi, wo_lo), (oT_lo, wo_hi)):
                        n += 1
                        last = nc.tensor.matmul(ps_y[:, :], a[:, t % 2, head], b[:, h, :], start=n == 1, stop=n == 3 * REP)
                last.then_inc(y_done, 1)

            def attention(G, with_next):
                for item in attention_order():
                    if item[0] == "S":
                        score(G, item[1], item[2])
                    elif item[0] == "C":
                        transpose_qk(G, item[1])
                    elif item[0] == "E":
                        transpose_probs(G, item[1])
                    elif item[0] == "PV":
                        values(G, item[1])
                    elif item[0] == "W":
                        project_out(G, item[1])
                    elif item[0] == "P" and with_next:
                        project(G + 1, item[1])

            def projections(G, after_attention):
                for item in projection_order(after_attention):
                    if item[0] == "P":
                        project(G, item[1])
                    elif item[0] == "C":
                        transpose_qk(G, item[1])
                    elif item[0] == "W":
                        project_out(G - 1, item[1])

            pe.wait_ge(const_loaded, 5 * 16)
            transpose_x(0)
            transpose_x(1)
            for item in projection_order(False):
                if item[0] == "P":
                    project(0, item[1])
                    if item[1] + 2 < TILES:
                        transpose_x(item[1] + 2)
                elif item[0] == "C":
                    transpose_qk(0, item[1])
            pe.wait_ge(const_made, 4)
            with pe.Fori(0, KV_HEADS - 1) as g:
                attention(g, True)
                projections(g + 1, True)
            attention(KV_HEADS - 1, False)
            project_out(KV_HEADS - 1, TILES - 1)

            pe.wait_ge(exp_done, UNITS * KV_HEADS)
            for i in range(NT):
                pe.wait_ge(w_above_done, i + 1)
                for r in range(4):
                    last = nc.tensor.matmul(ps_s[:, r // 2, (r % 2) * BANK:(r % 2 + 1) * BANK],
                                            eye_b[:, STEPS.index(STEP[i]), :],
                                            w_above[:, i % 2, r * DIM:(r + 1) * DIM],
                                            start=i == 0, stop=i == NT - 1)
                last.then_inc(w_sum_done, 1)
            pe.wait_ge(w_quant_done, 1)
            for kt in range(KT):
                if kt < 2:
                    pe.wait_ge(e_free, E_USES * KV_HEADS)
                else:
                    pe.wait_ge(wT_lo_done, kt - 1)
                for r in range(4):
                    last = nc.tensor.transpose(ps_e[:, kt % 2, r * P:(r + 1) * P], w_quant[:, r, kt * P:(kt + 1) * P],
                                               eye_f[:, :])
                last.then_inc(wT_done, 1)
            pe.wait_ge(wT_lo_done, KT)
            pe.wait_ge(y_added, TILES * KV_HEADS + 1)
            for t in range(TILES):
                pe.wait_ge(above_done, t + 1)
                if t:
                    pe.wait_ge(xgT_copied, t)
                for kt in range(KT):
                    for i in range(NT):
                        last = nc.tensor.matmul(ps_o[:, kt * P:(kt + 1) * P], above[:, i, kt * P:(kt + 1) * P],
                                                eye_b[:, 1, :], start=i == 0, stop=i == NT - 1)
                last.then_inc(xgT_done, 1)
                pe.wait_ge(xgT_copied, t + 1)
                if t:
                    pe.wait_ge(z_read, t)
                n = 0
                for kt in range(KT):
                    for w in (wT_hi, wT_lo):
                        n += 1
                        last = nc.tensor.matmul(ps_y[:, :], xg_T[:, kt * P:(kt + 1) * P], w[:, kt, :], start=n == 1,
                                                stop=n == 2 * KT)
                last.then_inc(z_done, 1)

        @block.scalar
        def _(act):
            def copy_x(t):
                act.wait_ge(xT_done, t + 1)
                bank = ps_o if t % 2 == 0 else ps_y
                nc.scalar.copy(xT_hi[:, :, t * P:(t + 1) * P], bank[:, :].rearrange("p (k s) -> p k s", k=KT)
                               ).then_inc(xT_hi_done, 1)

            def copy_v(G, t):
                act.wait_ge(rope_mul, TILES * G + t + 1)
                if t == 0 and not (isinstance(G, int) and G == 0):
                    act.wait_ge(pv_done, NB * G)
                nc.scalar.copy(v_hi[:, t, :], ps_s[:, t % 2, QKW:QKVW]).then_inc(v_hi_done, 1)

            def copy_qk(G, t):
                act.wait_ge(qkT_done, TILES * G + t + 1)
                rows = slice(t * P, (t + 1) * P)
                nc.scalar.copy(qT_hi[:, :, rows], ps_e[:, 0, :].rearrange("p (h s) -> p h s", h=REP))
                nc.scalar.copy(kT_hi[:, rows], ps_e[:, 1, 0:P]).then_inc(qkT_hi_done, 1)

            def exponentials(G, t, h):
                u = REP * t + h
                act.wait_ge(max_done, UNITS * G + u + 1)
                width = (t + 1) * P
                nc.scalar.activation(probs[t % 2][:, h, 0:width], ps_s[:, u % 2, 0:width], ACT.Exp,
                                     bias=neg_max[:, u % 8:u % 8 + 1],
                                     accum_out=row_sum[:, u % 8:u % 8 + 1]).then_inc(exp_done, 1)

            def copy_probs(G, b):
                act.wait_ge(pT_done, NB * G + b + 1)
                nc.scalar.copy(pT_hi[:, b % 2, :], ps_e[:, b % 2, :]).then_inc(pT_hi_done, 1)

            def copy_out(G, t):
                act.wait_ge(pv_done, NB * G + FIRST_BLOCK[t + 1])
                nc.scalar.copy(oT_hi[:, t % 2, :], ps_o[:, :]).then_inc(oT_hi_done, 1)

            def attention(G):
                waiting = None
                for item in attention_order():
                    if item[0] == "S":
                        if waiting:
                            exponentials(G, *waiting)
                        waiting = item[1:]
                    elif item[0] == "C":
                        copy_qk(G, item[1])
                    elif item[0] == "E":
                        copy_probs(G, item[1])
                    elif item[0] == "PV" and BLOCKS[item[1]][0] == BLOCKS[item[1]][1]:
                        copy_out(G, BLOCKS[item[1]][0])
                    elif item[0] == "P" and item[1] == 0:
                        exponentials(G, *waiting)
                        waiting = None

            def projections(G, after_attention):
                for item in projection_order(after_attention):
                    if item[0] == "V":
                        copy_v(G, item[1])
                    elif item[0] == "C":
                        copy_qk(G, item[1])

            copy_x(0)
            copy_x(1)
            for item in projection_order(False):
                if item[0] == "V":
                    copy_v(0, item[1])
                    if item[1] + 2 < TILES:
                        copy_x(item[1] + 2)
                elif item[0] == "C":
                    copy_qk(0, item[1])
            with act.Fori(0, KV_HEADS - 1) as g:
                attention(g)
                projections(g + 1, True)
            attention(KV_HEADS - 1)

            for kt in range(KT):
                act.wait_ge(wT_done, kt + 1)
                nc.scalar.copy(wT_hi[:, kt, :], ps_e[:, kt % 2, :]).then_inc(wT_hi_done, 1)
            for t in range(TILES):
                act.wait_ge(xgT_done, t + 1)
                if t:
                    act.wait_ge(z_done, t)
                nc.scalar.activation(xg_T, ps_o[:, :], ACT.Copy, bias=-GRID_MAX).then_inc(xgT_copied, 1)

        @block.gpsimd
        def _(pool):
            def inverse_root(n):
                pool.wait_ge(ln_var, n)
                nc.gpsimd.tensor_tensor(rstd[:, :], var_eps[:, :], minus_half[:, :], ALU.pow).then_inc(ln_rstd, 1)

            def split(G, c, hi, lo, src, signal):
                b = c % 2
                upto = 3 * 16 * (min(c, KT - 1) // 2 + 1) + 16 * max(0, (c - KT) // 2 + 1)
                pool.wait_ge(staged[b], STAGED * G + upto)
                pool.sem_inc(pool_turns, 1)
                nc.gpsimd.tensor_scalar(hi, src, 1.0, 1.0, ALU.mult, ALU.mult).then_inc(split_hi, 1)
                pool.wait_ge(split_hi, CHUNKS * G + c + 1)
                nc.gpsimd.tensor_tensor(lo, src, hi.bitcast(F32), ALU.subtract).then_inc(stage_free, 1)
                pool.wait_ge(stage_free, CHUNKS * G + c + 1)
                pool.sem_inc(signal, 1)

            def split_qkv(G, kt):
                if kt == 0 and not (isinstance(G, int) and G == 0):
                    pool.wait_ge(proj_done, TILES * G)
                split(G, kt, wqkv_hi[:, kt, :], wqkv_lo[:, kt, :], stage[:, kt % 2, :], wqkv_ready)

            def split_wo(G, h):
                if h == 0 and not (isinstance(G, int) and G == 0):
                    pool.wait_ge(y_done, TILES * G)
                split(G, KT + h, wo_hi[:, h, :], wo_lo[:, h, :], stage[:, h % 2, 0:DIM], wo_ready)

            def rotary_sum(G, t):
                pool.wait_ge(rope_mul, TILES * G + t + 1)
                s = t % 2
                nc.gpsimd.tensor_tensor(rope_a[:, s, :], rope_a[:, s, :], rope_b[:, s, :], ALU.add).then_inc(rope_sum, 1)

            def normalise(G, t, h):
                u = REP * t + h
                pool.wait_ge(inv_done, UNITS * G + u + 1)
                pool.sem_inc(pool_turns, 1)
                p = probs[t % 2][:, h, 0:(t + 1) * P]
                nc.gpsimd.tensor_scalar(p, p, row_inv[:, u % 8:u % 8 + 1], 1.0, ALU.mult, ALU.mult).then_inc(probs_ready, 1)

            def attention(G, with_next):
                for item in attention_order():
                    if item[0] == "S":
                        normalise(G, item[1], item[2])
                        if with_next and item[2] == REP - 1 and item[1] < KT:
                            split_qkv(G + 1, item[1])
                    elif item[0] == "P" and with_next:
                        rotary_sum(G + 1, item[1])

            nc.gpsimd.memset(minus_half[:, :], -0.5).then_inc(const_made, 1)
            nc.gpsimd.memset(y_acc[:, :, :], 0.0).then_inc(const_made, 1)
            pool.wait_ge(const_made, 1)
            inverse_root(1)
            for kt in range(2):
                split_qkv(0, kt)
            for t in range(1, TILES):
                inverse_root(t + 1)
                if t < 3:
                    split_qkv(0, t + 1)
                else:
                    rotary_sum(0, t - 3)
            for h in range(REP):
                rotary_sum(0, TILES - 3 + h) if h < 3 else None
                split_wo(0, h)
            with pool.Fori(0, KV_HEADS - 1) as g:
                attention(g, True)
                for t in range(2, TILES):
                    rotary_sum(g + 1, t)
                    if t >= TILES - REP:
                        split_wo(g + 1, t - (TILES - REP))
            attention(KV_HEADS - 1, False)
            for n in range(3 * TILES):
                inverse_root(TILES + n + 1)

        @block.vector
        def _(dve):
            step = [0]

            def chained(ins):
                step[0] += 1
                ins.then_inc(ln_step, 1)
                dve.wait_ge(ln_step, step[0])

            def statistics(src):
                chained(nc.vector.bn_stats(stats[:, :], src))
                chained(nc.vector.bn_aggr(mean_var[:, :], stats[:, :]))
                nc.vector.tensor_scalar(var_eps[:, :], mean_var[:, 1:2], LN_EPS, None, ALU.add).then_inc(ln_var, 1)

            def normalised(dst, src, n):
                dve.wait_ge(ln_rstd, n)
                return nc.vector.tensor_scalar(dst, src, mean_var[:, 0:1], rstd[:, :], ALU.subtract, ALU.mult)

            def layernorm_x(t):
                if t < 2:
                    dve.wait_ge(x_loaded[t], 16)
                statistics(x_sb[:, t, :])
                normalised(x_sb[:, t, :], x_sb[:, t, :], t + 1).then_inc(xn_ready, 1)

            def low_x(t):
                dve.wait_ge(xT_hi_done, t + 1)
                bank = ps_o if t % 2 == 0 else ps_y
                rows = slice(t * P, (t + 1) * P)
                nc.vector.tensor_tensor(xT_lo[:, :, rows], bank[:, :].rearrange("p (k s) -> p k s", k=KT),
                                        xT_hi[:, :, rows].bitcast(F32), ALU.subtract).then_inc(xT_lo_done, 1)

            def rotate(G, t):
                dve.wait_ge(proj_done, TILES * G + t + 1)
                s = t % 2
                qk = ps_s[:, s, 0:QKW].rearrange("p (h d r) -> p h d r", h=REP + 1, r=2)
                pair = qk[:, :, :, ::-1]
                shape = [P, REP + 1, P // 2, 2]
                c = cos_t[:, t, :].rearrange("p (a d b) -> p a d b", a=1, b=1).to_broadcast(shape)
                sn = sin_t[:, t, :].rearrange("p (a d r) -> p a d r", a=1, r=2).to_broadcast(shape)
                nc.vector.tensor_tensor(rope_a[:, s, :].rearrange("p (h d r) -> p h d r", h=REP + 1, r=2), qk, c, ALU.mult)
                nc.vector.tensor_tensor(rope_b[:, s, :].rearrange("p (h d r) -> p h d r", h=REP + 1, r=2), pair, sn,
                                        ALU.mult).then_inc(rope_mul, 1)

            def low_v(G, t):
                dve.wait_ge(v_hi_done, TILES * G + t + 1)
                nc.vector.tensor_tensor(v_lo[:, t, :], ps_s[:, t % 2, QKW:QKVW], v_hi[:, t, :].bitcast(F32),
                                        ALU.subtract).then_inc(qkv_free, 1)

            def low_qk(G, t):
                dve.wait_ge(qkT_hi_done, TILES * G + t + 1)
                rows = slice(t * P, (t + 1) * P)
                nc.vector.tensor_tensor(qT_lo[:, :, rows], ps_e[:, 0, :].rearrange("p (h s) -> p h s", h=REP),
                                        qT_hi[:, :, rows].bitcast(F32), ALU.subtract).then_inc(e_free, 1)
                nc.vector.tensor_tensor(kT_lo[:, rows], ps_e[:, 1, 0:P], kT_hi[:, rows].bitcast(F32),
                                        ALU.subtract).then_inc(e_free, 1)

            def row_max(G, t, h):
                u = REP * t + h
                dve.wait_ge(scores_done, UNITS * G + u + 1)
                nc.vector.tensor_reduce(neg_max[:, u % 8:u % 8 + 1], ps_s[:, u % 2, 0:(t + 1) * P], AX.X, ALU.max,
                                        negate=True).then_inc(max_done, 1)

            def row_inverse(G, u):
                dve.wait_ge(exp_done, UNITS * G + u + 1)
                nc.vector.reciprocal(row_inv[:, u % 8:u % 8 + 1], row_sum[:, u % 8:u % 8 + 1]).then_inc(inv_done, 1)

            def low_probs(G, b):
                dve.wait_ge(pT_hi_done, NB * G + b + 1)
                nc.vector.tensor_tensor(pT_lo[:, b % 2, :], ps_e[:, b % 2, :], pT_hi[:, b % 2, :].bitcast(F32),
                                        ALU.subtract).then_inc(e_free, 1)

            def low_out(G, t):
                dve.wait_ge(oT_hi_done, TILES * G + t + 1)
                nc.vector.tensor_tensor(oT_lo[:, t % 2, :], ps_o[:, :], oT_hi[:, t % 2, :].bitcast(F32),
                                        ALU.subtract).then_inc(oT_lo_done, 1)

            def add_y(G, t):
                dve.wait_ge(y_done, TILES * G + t + 1)
                nc.vector.tensor_tensor(y_acc[:, t, :], ps_y[:, :], y_acc[:, t, :], ALU.add).then_inc(y_added, 1)

            def attention(G, with_next):
                for item in attention_order():
                    if item[0] == "S":
                        u = REP * item[1] + item[2]
                        row_max(G, item[1], item[2])
                        if u:
                            row_inverse(G, u - 1)
                    elif item[0] == "C":
                        low_qk(G, item[1])
                    elif item[0] == "E":
                        low_probs(G, item[1])
                    elif item[0] == "PV" and BLOCKS[item[1]][0] == BLOCKS[item[1]][1]:
                        low_out(G, BLOCKS[item[1]][0])
                    elif item[0] == "W":
                        add_y(G, item[1])
                    elif item[0] == "P":
                        if item[1] == 0:
                            row_inverse(G, UNITS - 1)
                        if with_next:
                            rotate(G + 1, item[1])

            def projections(G, after_attention):
                for item in projection_order(after_attention):
                    if item[0] == "P":
                        rotate(G, item[1])
                    elif item[0] == "V":
                        low_v(G, item[1])
                    elif item[0] == "C":
                        low_qk(G, item[1])
                    elif item[0] == "W":
                        add_y(G - 1, item[1])

            dve.sem_inc(oT_lo_done, 1)
            dve.sem_inc(y_added, 1)
            dve.wait_ge(const_made, 2)
            layernorm_x(0)
            dve.wait_ge(const_loaded, 5 * 16)
            for i, s in enumerate(STEPS):
                last = nc.vector.tensor_scalar(eye_b[:, i, :], eye_f[:, :], s, None, ALU.mult)
            last.then_inc(const_made, 1)
            nc.vector.tensor_copy(causal_b[:, :], causal_f).then_inc(const_made, 1)
            dve.wait_ge(const_made, 4)
            layernorm_x(1)
            low_x(0)
            layernorm_x(2)
            low_x(1)
            for item in projection_order(False):
                if item[0] == "P":
                    rotate(0, item[1])
                elif item[0] == "V":
                    low_v(0, item[1])
                    if item[1] + 3 < TILES:
                        layernorm_x(item[1] + 3)
                    if item[1] + 2 < TILES:
                        low_x(item[1] + 2)
                elif item[0] == "C":
                    low_qk(0, item[1])
            with dve.Fori(0, KV_HEADS - 1) as g:
                attention(g, True)
                projections(g + 1, True)
            attention(KV_HEADS - 1, False)
            add_y(KV_HEADS - 1, TILES - 1)

            def grid_scale(n):
                a, q, e = s_max[:, 0:n], s_q[:, 0:n], s_e[:, 0:n]
                chained(nc.vector.tensor_scalar(q, a, 1.0 / GRID_MAX, None, ALU.mult))
                chained(nc.vector.scalar_tensor_tensor(e, q, -4.0, a, ALU.mult, ALU.add))
                chained(nc.vector.scalar_tensor_tensor(e, q, -2.0, e, ALU.mult, ALU.add))
                chained(nc.vector.scalar_tensor_tensor(scale[:, 0:n], e, 1.0 / GRID_MAX, q, ALU.mult, ALU.add))

            dve.wait_ge(ffn_loaded, 3 * 16)
            groups = w_raw[:, :, :].rearrange("p r (k i) -> p (r k) i", k=KT)
            chained(nc.vector.tensor_reduce(s_max[:, 0:16], groups, AX.X, ALU.max, apply_absolute_value=True))
            grid_scale(16)
            for i in range(NT):
                if i >= 2:
                    dve.wait_ge(w_sum_done, i - 1)
                thr_w = (s_q, s_e)[i % 2]
                chained(nc.vector.tensor_scalar(thr_w[:, :], scale[:, 0:16], THRESHOLD[i], None, ALU.mult))
                nc.vector.tensor_tensor(w_above[:, i % 2, :].rearrange("p (k i) -> p k i", k=16), groups,
                                        thr_w[:, :].rearrange("p (k i) -> p k i", i=1).to_broadcast([P, 16, P]),
                                        ALU.is_gt).then_inc(w_above_done, 1)
            dve.wait_ge(w_sum_done, NT)
            for r in range(4):
                last = nc.vector.scalar_tensor_tensor(
                    w_quant[:, r, :].rearrange("p (k i) -> p k i", k=KT),
                    ps_s[:, r // 2, (r % 2) * BANK:(r % 2 + 1) * BANK].rearrange("p (k i) -> p k i", k=KT), -GRID_MAX,
                    scale[:, r * KT:(r + 1) * KT].rearrange("p (k i) -> p k i", i=1).to_broadcast([P, KT, P]),
                    ALU.add, ALU.mult)
            last.then_inc(w_quant_done, 1)
            for kt in range(KT):
                dve.wait_ge(wT_hi_done, kt + 1)
                nc.vector.tensor_tensor(wT_lo[:, kt, :], ps_e[:, kt % 2, :], wT_hi[:, kt, :].bitcast(F32),
                                        ALU.subtract).then_inc(wT_lo_done, 1)
            n = TILES
            for t in range(TILES):
                y = y_acc[:, t, :]
                statistics(y)
                n += 1
                chained(normalised(y, y, n))
                chained(nc.vector.tensor_tensor(y, y, x_sb[:, t, :], ALU.add))
                statistics(y)
                n += 1
                chained(normalised(xn2, y, n))
                chained(nc.vector.tensor_scalar(xn2, xn2, CLIP, -CLIP, ALU.min, ALU.max))
                chained(nc.vector.tensor_reduce(s_max[:, 0:1], xn2, AX.X, ALU.max, apply_absolute_value=True))
                grid_scale(1)
                chained(nc.vector.tensor_scalar(thr_s[:, :], thr[:, :], scale[:, 0:1], None, ALU.mult))
                if t:
                    dve.wait_ge(xgT_done, t)
                for i in range(NT):
                    last = nc.vector.tensor_scalar(above[:, i, :], xn2, thr_s[:, i:i + 1], STEP[i], ALU.is_gt, ALU.mult)
                last.then_inc(above_done, 1)
                dve.wait_ge(z_done, t + 1)
                nc.vector.scalar_tensor_tensor(z_sb, ps_y[:, :], scale[:, 0:1], bias_b, ALU.mult, ALU.add).then_inc(z_read, 1)
                dve.wait_ge(z_read, t + 1)
                statistics(z_sb)
                n += 1
                chained(normalised(z_sb, z_sb, n))
                if t >= 2:
                    dve.wait_ge(stored[t % 2], 16 * (t // 2))
                nc.vector.tensor_tensor(res[:, t % 2, :], z_sb, y, ALU.add).then_inc(res_ready, 1)


_INS = ["L0_attn_x", "L0_attn_wq", "L0_attn_wk", "L0_attn_wv", "L0_attn_wo", "L0_ffn_weight", "L0_ffn_bias"]
_OUTS = [((1, SEQ, DIM), "float32")]


def kernel(**inputs):
    import numpy as _np
    import concourse.bacc as _bacc
    from concourse import mybir as _mybir
    from concourse.bass_utils import run_bass_kernel_spmd as _run

    nc = _bacc.Bacc("TRN2", target_bir_lowering=False, num_devices=1)
    arrays, args = {}, []
    given = [(name, _np.ascontiguousarray(inputs[name])) for name in _INS]
    given += list(shape_constants().items())
    for name, a in given:
        arrays[f"in_{name}_dram"] = a
        args.append(nc.dram_tensor(f"in_{name}_dram", a.shape, _mybir.dt.from_np(a.dtype), kind="ExternalInput").ap())
    for i, (shape, dtype) in enumerate(_OUTS):
        dt = _mybir.dt.from_np(_np.dtype(dtype))
        args.append(nc.dram_tensor(f"out_{i}_dram", shape, dt, kind="ExternalOutput").ap())
    sandwich_kernel(nc, *args)
    r = _run(nc, [arrays], core_ids=[0])
    got = tuple(r.results[0][f"out_{i}_dram"] for i in range(len(_OUTS)))
    return got[0]
```
